# Optimizing a Trainium2 kernel written in Bass

```python
import numpy as np
import jax
import jax.numpy as jnp

def _softmax(x, axis=-1):
    return jax.nn.softmax(x, axis=axis)

def _gelu(x):
    return jax.nn.gelu(x, approximate=True)

def _silu(x):
    return jax.nn.silu(x)

def _sigmoid(x):
    return jax.nn.sigmoid(x)

def _layernorm(x, axis=-1, eps=1e-05):
    m = jnp.mean(x, axis=axis, keepdims=True)
    v = jnp.var(x, axis=axis, keepdims=True)
    return (x - m) / jnp.sqrt(v + eps)

def _scatter_add(tgt, idx, src, axis=0):
    return tgt.at[idx].add(src)

def _segment_sum(src, seg, n):
    return jax.ops.segment_sum(src, seg, n)
kernel_name = 'mk_gps_d1_gnn_r32_4bac02'

def setup_inputs(seed: int=0):
    np.random.seed(seed)
    _w = jnp.asarray

    def _rec_inputs():
        import jax
        import jax.numpy as jnp
        _gk = jax.random.key(seed)
        x = -0.0003713 + 1 * jax.random.normal(jax.random.fold_in(_gk, 1), (3125, 256), jnp.float32)
        src = jax.random.randint(jax.random.fold_in(_gk, 2), (50000,), 0, 3125, jnp.int32)
        dst = jnp.minimum((3125 * jax.random.uniform(jax.random.fold_in(_gk, 3), (50000,)) ** 2.0).astype(jnp.int32), 99999)
        _o = jnp.argsort(dst, stable=True)
        src = src[_o]
        dst = dst[_o]
        return (x, src, dst)
    x, src, dst = _rec_inputs()

    def _L0_gnn_setup():
        import jax, jax.numpy as jnp
        import numpy as np
        from jax.ops import segment_sum, segment_max
        N_NODES = 50000
        N_EDGES = 25000
        IN_DIM = 256
        OUT_DIM = 64
        N_HEADS = 4
        key = jax.random.key(seed)
        k1, k2, k3, k4, k5, k6 = jax.random.split(key, 6)
        h = jax.random.normal(k1, (N_NODES, IN_DIM), dtype=jnp.float32)
        src = jax.random.randint(k2, (N_EDGES,), 0, N_NODES, dtype=jnp.int32)
        dst = jax.random.randint(k3, (N_EDGES,), 0, N_NODES, dtype=jnp.int32)
        W = jax.random.normal(k4, (N_HEADS, IN_DIM, OUT_DIM), dtype=jnp.float32) * 0.05
        a_src = jax.random.normal(k5, (N_HEADS, OUT_DIM), dtype=jnp.float32) * 0.05
        a_dst = jax.random.normal(k6, (N_HEADS, OUT_DIM), dtype=jnp.float32) * 0.05
        return {'h': h, 'src': src, 'dst': dst, 'W': W, 'a_src': a_src, 'a_dst': a_dst}
    _L0_gnn_all = _L0_gnn_setup()
    _L0_gnn_in = {k: v for k, v in _L0_gnn_all.items() if k in ('W', 'a_src', 'a_dst')}
    del _L0_gnn_all

    def _L0_mix_setup():
        import jax, jax.numpy as jnp
        import numpy as np
        DIM = 256
        HEADS = 4
        HEAD_DIM = DIM // HEADS
        MLP_HIDDEN = DIM * 3
        B, N = (8, 128)
        EPS = 1e-05

        def _layernorm(x, g, b):
            mu = jnp.mean(x, axis=-1, keepdims=True)
            var = jnp.mean(jnp.square(x - mu), axis=-1, keepdims=True)
            return (x - mu) * jax.lax.rsqrt(var + EPS) * g + b
        key = jax.random.key(seed)
        ks = jax.random.split(key, 8)
        s = 0.02
        return {'x': jax.random.normal(ks[0], (B, N, DIM), dtype=jnp.float32), 'w_qkv': jax.random.normal(ks[1], (DIM, 3 * DIM), dtype=jnp.float32) * s, 'b_qkv': jnp.zeros((3 * DIM,), dtype=jnp.float32), 'norm_g': jnp.ones((DIM,), dtype=jnp.float32), 'norm_b': jnp.zeros((DIM,), dtype=jnp.float32), 'w_fc1': jax.random.normal(ks[2], (DIM, MLP_HIDDEN), dtype=jnp.float32) * s, 'b_fc1': jnp.zeros((MLP_HIDDEN,), dtype=jnp.float32), 'w_fc2': jax.random.normal(ks[3], (MLP_HIDDEN, DIM), dtype=jnp.float32) * s, 'b_fc2': jnp.zeros((DIM,), dtype=jnp.float32)}
    _L0_mix_all = _L0_mix_setup()
    _L0_mix_in = {k: v for k, v in _L0_mix_all.items() if k in ('w_qkv', 'b_qkv', 'norm_g', 'norm_b', 'w_fc1', 'b_fc1', 'w_fc2', 'b_fc2')}
    del _L0_mix_all

    def _L0_ffn_setup():
        import jax, jax.numpy as jnp
        import numpy as np
        E = 8
        K = 2
        D = 256
        H = 512
        DOUT = 256
        EPS = 1e-05
        key = jax.random.key(seed)
        ks = jax.random.split(key, 9)
        s = 0.02
        return {'x': jax.random.normal(ks[0], (4, 256, D), jnp.float32), 'gamma': 1.0 + 0.05 * jax.random.normal(ks[1], (D,), jnp.float32), 'beta': 0.05 * jax.random.normal(ks[2], (D,), jnp.float32), 'Wr': 0.01 * jax.random.normal(ks[3], (D, E), jnp.float32), 'br': jnp.zeros((E,), jnp.float32), 'W1': s * jax.random.normal(ks[4], (E, D, H), jnp.float32), 'b1': s * jax.random.normal(ks[5], (E, H), jnp.float32), 'W2': s * jax.random.normal(ks[6], (E, H, DOUT), jnp.float32), 'b2': s * jax.random.normal(ks[7], (E, DOUT), jnp.float32)}
    _L0_ffn_all = _L0_ffn_setup()
    _L0_ffn_in = {k: v for k, v in _L0_ffn_all.items() if k in ('gamma', 'beta', 'Wr', 'br', 'W1', 'b1', 'W2', 'b2')}
    del _L0_ffn_all
    return {'x': x, 'src': src, 'dst': dst, 'L0_gnn_W': _L0_gnn_in['W'], 'L0_gnn_a_src': _L0_gnn_in['a_src'], 'L0_gnn_a_dst': _L0_gnn_in['a_dst'], 'L0_mix_w_qkv': _L0_mix_in['w_qkv'], 'L0_mix_b_qkv': _L0_mix_in['b_qkv'], 'L0_mix_norm_g': _L0_mix_in['norm_g'], 'L0_mix_norm_b': _L0_mix_in['norm_b'], 'L0_mix_w_fc1': _L0_mix_in['w_fc1'], 'L0_mix_b_fc1': _L0_mix_in['b_fc1'], 'L0_mix_w_fc2': _L0_mix_in['w_fc2'], 'L0_mix_b_fc2': _L0_mix_in['b_fc2'], 'L0_ffn_gamma': _L0_ffn_in['gamma'], 'L0_ffn_beta': _L0_ffn_in['beta'], 'L0_ffn_Wr': _L0_ffn_in['Wr'], 'L0_ffn_br': _L0_ffn_in['br'], 'L0_ffn_W1': _L0_ffn_in['W1'], 'L0_ffn_b1': _L0_ffn_in['b1'], 'L0_ffn_W2': _L0_ffn_in['W2'], 'L0_ffn_b2': _L0_ffn_in['b2']}

def reference(x, src, dst, L0_gnn_W, L0_gnn_a_src, L0_gnn_a_dst, L0_mix_w_qkv, L0_mix_b_qkv, L0_mix_norm_g, L0_mix_norm_b, L0_mix_w_fc1, L0_mix_b_fc1, L0_mix_w_fc2, L0_mix_b_fc2, L0_ffn_gamma, L0_ffn_beta, L0_ffn_Wr, L0_ffn_br, L0_ffn_W1, L0_ffn_b1, L0_ffn_W2, L0_ffn_b2):
    import jax
    import jax.numpy as jnp

    def _L0_gnn_ref(h, src, dst, W, a_src, a_dst):
        import jax, jax.numpy as jnp
        import numpy as np
        from jax.ops import segment_sum, segment_max
        N_NODES = 50000
        N_EDGES = 25000
        IN_DIM = 256
        OUT_DIM = 64
        N_HEADS = 4
        n = h.shape[0]
        z = jnp.einsum('ni,hio->nho', h, W)
        e_src = jnp.einsum('nho,ho->nh', z, a_src)
        e_dst = jnp.einsum('nho,ho->nh', z, a_dst)
        e = jax.nn.leaky_relu(e_src[src] + e_dst[dst], negative_slope=0.01)
        m = segment_max(e, dst, num_segments=n)
        e_exp = jnp.exp(e - m[dst])
        denom = segment_sum(e_exp, dst, num_segments=n)
        alpha = e_exp / denom[dst]
        msg = alpha[:, :, None] * z[src]
        out = segment_sum(msg, dst, num_segments=n)
        return out.reshape(n, N_HEADS * OUT_DIM)

    def _L0_mix_ref(x, w_qkv, b_qkv, norm_g, norm_b, w_fc1, b_fc1, w_fc2, b_fc2):
        import jax, jax.numpy as jnp
        import numpy as np
        DIM = 256
        HEADS = 4
        HEAD_DIM = DIM // HEADS
        MLP_HIDDEN = DIM * 3
        B, N = (8, 128)
        EPS = 1e-05

        def _layernorm(x, g, b):
            mu = jnp.mean(x, axis=-1, keepdims=True)
            var = jnp.mean(jnp.square(x - mu), axis=-1, keepdims=True)
            return (x - mu) * jax.lax.rsqrt(var + EPS) * g + b
        Bx, Nx, C = x.shape
        scale = HEAD_DIM ** (-0.5)
        qkv = (x @ w_qkv + b_qkv).reshape(Bx, Nx, 3, HEADS, HEAD_DIM)
        qkv = jnp.transpose(qkv, (2, 0, 3, 1, 4))
        q, k, v = (qkv[0], qkv[1], qkv[2])
        k = k * scale
        attn = jnp.einsum('bhnd,bhne->bhde', k, v)
        attn = jax.nn.softmax(attn, axis=-1)
        xf = jnp.einsum('bhde,bhne->bhnd', attn, q)
        xf = jnp.transpose(xf, (0, 2, 1, 3)).reshape(Bx, Nx, C)
        x = x + xf
        h = _layernorm(x, norm_g, norm_b)
        h = jax.nn.gelu(h @ w_fc1 + b_fc1, approximate=False) @ w_fc2 + b_fc2
        return x + h

    def _L0_ffn_ref(x, gamma, beta, Wr, br, W1, b1, W2, b2):
        import jax, jax.numpy as jnp
        import numpy as np
        E = 8
        K = 2
        D = 256
        H = 512
        DOUT = 256
        EPS = 1e-05
        mu = jnp.mean(x, axis=-1, keepdims=True)
        var = jnp.mean(jnp.square(x - mu), axis=-1, keepdims=True)
        xn = (x - mu) * jax.lax.rsqrt(var + EPS) * gamma + beta
        logits = jnp.einsum('bsd,de->bse', xn, Wr) + br
        top_vals, top_idx = jax.lax.top_k(logits, K)
        w = jax.nn.softmax(top_vals, axis=-1)
        w_full = jnp.einsum('bsk,bske->bse', w, jax.nn.one_hot(top_idx, E, dtype=w.dtype))
        y = jnp.zeros(x.shape[:-1] + (DOUT,), x.dtype)
        for e in range(E):
            h = jax.nn.gelu(jnp.einsum('bsd,dh->bsh', xn, W1[e]) + b1[e], approximate=False)
            y_e = jnp.einsum('bsh,hd->bsd', h, W2[e]) + b2[e]
            y = y + y_e * w_full[..., e, None]
        return y
    xn = _layernorm(x, axis=-1)
    x = x + _L0_gnn_ref(xn, src, dst, L0_gnn_W, L0_gnn_a_src, L0_gnn_a_dst) + _L0_mix_ref(xn[None], L0_mix_w_qkv, L0_mix_b_qkv, L0_mix_norm_g, L0_mix_norm_b, L0_mix_w_fc1, L0_mix_b_fc1, L0_mix_w_fc2, L0_mix_b_fc2)[0]
    x = x + _L0_ffn_ref(_layernorm(x, axis=-1)[None], L0_ffn_gamma, L0_ffn_beta, L0_ffn_Wr, L0_ffn_br, L0_ffn_W1, L0_ffn_b1, L0_ffn_W2, L0_ffn_b2)[0]
    return x

_drawn_inputs = setup_inputs


def setup_inputs(seed=0):
    import zlib

    import numpy as np

    out = dict(_drawn_inputs(seed))
    spreads = {'L0_mix_b_qkv': (0.0, 0.1),
     'L0_mix_norm_g': (1.0, 0.6),
     'L0_mix_norm_b': (0.0, 0.8),
     'L0_mix_b_fc1': (0.0, 0.548),
     'L0_mix_b_fc2': (0.0, 0.1),
     'L0_ffn_br': (0.0, 0.294)}
    factors = {'L0_gnn_a_dst': 4.459,
     'L0_ffn_gamma': 8.0,
     'L0_ffn_beta': 8.0,
     'L0_ffn_Wr': 2.979,
     'L0_ffn_b1': 21.649,
     'L0_ffn_b2': 8.0}
    for name, (base, spread) in spreads.items():
        noise = np.random.default_rng([zlib.crc32(name.encode()), seed]).standard_normal(out[name].shape)
        drawn = base * np.exp(spread * noise) if base else spread * noise
        out[name] = jnp.asarray(drawn.astype(out[name].dtype))
    for name, factor in factors.items():
        out[name] = (out[name] * factor).astype(out[name].dtype)
    return out
```

```python
from contextlib import ExitStack

import concourse.bass as bass
from concourse import mybir

ALU = mybir.AluOpType
ACT = mybir.ActivationFunctionType
AX = mybir.AxisListType
F32 = mybir.dt.float32
I32 = mybir.dt.int32
EPS = 1e-5
BIG = 1e30
SLOPE = 0.01
ds = bass.ds


def at(buf, t, width=None):
    return buf[:, ds(t, 1), :].rearrange("p a c -> p (a c)")


def wait_ge(eng, sem, count):
    eng.wait_ge(sem, count)


def wait_apart(eng, sem, count):
    eng.wait_ge(sem, count)
    eng.nop(nofuse=True)


def in_order(eng, sem, base=0):
    n = [0]

    def step(ins, wait=True, apart=False):
        n[0] += 1
        ins.then_inc(sem, 1)
        if wait:
            (wait_apart if apart else wait_ge)(eng, sem, base + n[0])

    return step


def gps_layer_kernel(nc, x, src, dst, gnn_W, gnn_a_src, gnn_a_dst, w_qkv, b_qkv, norm_g, norm_b,
                     w_fc1, b_fc1, w_fc2, b_fc2, gamma, beta, Wr, br, W1, b1, W2, b2, out):
    N, D = x.shape
    E = src.shape[0]
    HEADS, _, HD = gnn_W.shape
    ROWS = 125
    TILES = N // ROWS
    CHUNKS = E // ROWS
    assert TILES * ROWS == N and CHUNKS * ROWS == E and D == 256 and HEADS * HD == D
    SLOTS = 5
    ROUNDS = TILES // SLOTS
    KD = D // 128
    ZW = HD + 1
    ZROW = HEADS * ZW
    MLP = w_fc1.shape[1]
    MB = MLP // 128
    EXPERTS, _, HID = W1.shape
    HB = HID // 128

    z_table = nc.dram_tensor("z_table", (N, ZROW), F32).ap()
    es_table = nc.dram_tensor("es_table", (N, HEADS), F32).ap()
    ed_table = nc.dram_tensor("ed_table", (N, HEADS), F32).ap()
    xn_dram = nc.dram_tensor("xn_dram", (N, D), F32).ap()

    def rows_of(dram, t):
        return dram[ds(t * ROWS, ROWS), :]

    with ExitStack() as top:
        top.enter_context(nc.allow_non_contiguous_dma(reason="small vectors turned onto partitions"))
        def sem(name):
            return top.enter_context(nc.semaphore(name))

        def sb(stack, name, shape, dt=F32):
            return stack.enter_context(nc.sbuf_tensor(name, shape, dt))

        def bank(stack, name, shape=(128, 512)):
            return stack.enter_context(nc.psum_tensor(name, list(shape), F32))

        ident = sb(top, "ident", [128, 128])
        total = sb(top, "total", [ROWS, TILES, D])
        src_i = sb(top, "src_i", [ROWS, CHUNKS], I32)
        dst_i = sb(top, "dst_i", [ROWS, CHUNKS], I32)
        dst_f = sb(top, "dst_f", [ROWS, CHUNKS])
        kv_sum = sb(top, "kv_sum", [128, D])

        ident_zeroed = sem("ident_zeroed")
        ident_ready = sem("ident_ready")
        dve_steps = sem("dve_steps")

        with ExitStack() as st:
            xs = [sb(st, f"xs{j}", [ROWS, D]) for j in range(SLOTS)]
            xn = [sb(st, f"xn{j}", [ROWS, D]) for j in range(SLOTS)]
            xT = [sb(st, f"xT{j}", [128, KD, ROWS]) for j in range(SLOTS)]
            zrow = [sb(st, f"zrow{j}", [ROWS, HEADS, ZW]) for j in range(SLOTS)]
            kv = [sb(st, f"kv{j}", [ROWS, 2 * D]) for j in range(SLOTS)]
            wz = sb(st, "wz", [128, KD, D + 2 * HEADS])
            a_b = sb(st, "a_b", [128, 2, D])
            a_prod = sb(st, "a_prod", [128, 2 * KD, D])
            wkv = sb(st, "wkv", [128, KD, 2 * D])
            bkv = sb(st, "bkv", [ROWS, 2 * D])
            stats = sb(st, "stats", [ROWS, SLOTS, 6])
            mv = sb(st, "mv", [ROWS, SLOTS, 2])
            veps = sb(st, "veps", [ROWS, SLOTS])
            std = sb(st, "std", [ROWS, SLOTS])
            rstd = sb(st, "rstd", [ROWS, SLOTS])
            esed = sb(st, "esed", [ROWS, TILES, 2 * HEADS])
            EB = 4
            EC = CHUNKS // EB
            e_raw = sb(st, "e_raw", [EC, 2, EB, ROWS], I32)
            e_f = sb(st, "e_f", [EC, 2, EB, ROWS])
            wait_carrier = sb(st, "wait_carrier", [ROWS, 1])
            zero_w = sb(st, "zero_w", [128, 128])
            tp = [bank(st, f"tp{b}") for b in range(2)]
            zp = [bank(st, f"zp{b}") for b in range(2)]
            kvp = [bank(st, f"kvp{b}") for b in range(2)]
            kvs = bank(st, "kvs")
            ep = bank(st, "ep")

            x_in = [sem(f"x_in{j}") for j in range(SLOTS)]
            gw_in, mixw_in, edges_in = sem("gw_in"), sem("mixw_in"), sem("edges_in")
            ones_ready = sem("ones_ready")
            veps_ready, std_ready, normed = sem("veps_ready"), sem("std_ready"), sem("normed")
            turned, xT_ready = sem("turned"), sem("xT_ready")
            z_done, z_out_ready, esed_ready = sem("z_done"), sem("z_out_ready"), sem("esed_ready")
            kv_done, kv_ready, kvs_done = sem("kv_done"), sem("kv_ready"), sem("kvs_done")
            z_stored = [sem(f"z_stored{j}") for j in range(SLOTS)]
            xn_stored = [sem(f"xn_stored{j}") for j in range(SLOTS)]
            wz_ready, zero_ready = sem("wz_ready"), sem("zero_ready")
            ef_ready, e_turned, e_taken = sem("ef_ready"), sem("e_turned"), sem("e_taken")
            kvs_taken, tables_stored = sem("kvs_taken"), sem("tables_stored")

            def bank_free(t, j):
                return t if j == 0 else t - 1

            with nc.Block() as block:
                @block.sync
                def _(sp):
                    def load(t, j):
                        sp.dma_start(xs[j][:], rows_of(x, t)).then_inc(x_in[j], 16)

                    for j in range(SLOTS):
                        load(j, j)
                    for k in range(KD):
                        sp.dma_start(wz[:, k, 0:D].rearrange("p (h o) -> p h o", h=HEADS),
                                     gnn_W[:, k * 128:(k + 1) * 128, :].rearrange("h i o -> i h o")
                                     ).then_inc(gw_in, 16)
                    for s, a in enumerate((gnn_a_src, gnn_a_dst)):
                        sp.dma_start(a_b[:, s, :], a.rearrange("h o -> (h o)").partition_broadcast(128)
                                     ).then_inc(gw_in, 16)
                    sp.dma_start(wkv[:], w_qkv[:, D:3 * D].rearrange("(k p) c -> p k c", p=128)
                                 ).then_inc(mixw_in, 16)
                    sp.dma_start(bkv[:], b_qkv[D:3 * D].partition_broadcast(ROWS)).then_inc(mixw_in, 16)
                    for s, e in enumerate((src, dst)):
                        sp.dma_start(e_raw[:, s], e.rearrange("(b p e) -> p b e", b=EB, p=EC)
                                     ).then_inc(edges_in, 16)
                    with sp.Fori(1, ROUNDS) as i:
                        for j in range(SLOTS):
                            sp.wait_ge(normed, i * SLOTS + j - SLOTS + 1)
                            load(i * SLOTS + j, j)
                    sp.wait_ge(esed_ready, TILES)
                    for s, table in enumerate((es_table, ed_table)):
                        sp.dma_start(table.rearrange("(t p) h -> p t h", p=ROWS),
                                     esed[:, :, s * HEADS:(s + 1) * HEADS]).then_inc(tables_stored, 16)
                    sp.wait_ge(tables_stored, 32)

                @block.gpsimd
                def _(pool):
                    pool.memset(ident[:], 0.0).then_inc(ident_zeroed, 1)
                    pool.wait_ge(ident_zeroed, 1)
                    pool.affine_select(out=ident[:], in_=ident[:], compare_op=ALU.not_equal, fill=1.0,
                                       base=0, pattern=[[-1, 128]], channel_multiplier=1
                                       ).then_inc(ident_ready, 1)
                    for j in range(SLOTS):
                        pool.memset(zrow[j][:, :, HD:ZW], 1.0).then_inc(ones_ready, 1)
                    pool.memset(zero_w[:], 0.0).then_inc(zero_ready, 1)
                    with pool.Fori(0, ROUNDS) as i:
                        for j in range(SLOTS):
                            t = i * SLOTS + j
                            pool.wait_ge(normed, t + 1)
                            pool.dma_start(rows_of(xn_dram, t), xn[j][:]).then_inc(xn_stored[j], 16)
                            pool.wait_ge(z_out_ready, t + 1)
                            pool.dma_start(rows_of(z_table, t), zrow[j][:].rearrange("p h c -> p (h c)")
                                           ).then_inc(z_stored[j], 16)
                    for j in range(SLOTS):
                        pool.wait_ge(xn_stored[j], 16 * ROUNDS)
                        pool.wait_ge(z_stored[j], 16 * ROUNDS)

                @block.vector
                def _(dve):
                    step = in_order(dve, dve_steps)
                    dve.wait_ge(gw_in, 64)
                    for s in range(2):
                        for k in range(KD):
                            step(dve.tensor_tensor(a_prod[:, s * KD + k, :], wz[:, k, 0:D],
                                                   a_b[:, s, :], ALU.mult))
                            ins = dve.tensor_reduce(wz[:, k, D + s * HEADS:D + (s + 1) * HEADS],
                                                    a_prod[:, s * KD + k, :].rearrange("p (h o) -> p h o", h=HEADS),
                                                    AX.X, ALU.add)
                    ins.then_inc(wz_ready, 1)
                    dve.wait_ge(mixw_in, 32)
                    pre = 2 * KD
                    PER = 2 * SLOTS + 1
                    with dve.Fori(0, ROUNDS) as i:
                        step = in_order(dve, dve_steps, pre + PER * i)
                        for j in range(SLOTS):
                            dve.wait_ge(x_in[j], 16 * i + 16)
                            step(dve.bn_stats(stats[:, j, :], xs[j][:]), wait=j == SLOTS - 1)
                        dve.memset(wait_carrier[:], 0.0)
                        for j in range(SLOTS):
                            step(dve.bn_aggr(mv[:, j, :], stats[:, j, :]), wait=j == SLOTS - 1)
                        dve.tensor_scalar(veps[:], mv[:, :, 1], EPS, None, ALU.add).then_inc(veps_ready, 1)
                        dve.wait_ge(std_ready, i + 1)
                        step(dve.reciprocal(rstd[:], std[:]))
                        dve.wait_ge(turned, SLOTS * i)
                        for j in range(SLOTS):
                            dve.wait_ge(xn_stored[j], 16 * i)
                            dve.tensor_scalar(xn[j][:], xs[j][:], mv[:, j, 0:1], rstd[:, j:j + 1],
                                              ALU.subtract, ALU.mult).then_inc(normed, 1)
                        for j in range(SLOTS):
                            t = i * SLOTS + j
                            dve.wait_ge(kv_done, t + 1)
                            dve.tensor_tensor(kv[j][:], kvp[j % 2][0:ROWS, :], bkv[:], ALU.add
                                              ).then_inc(kv_ready, 1)
                    dve.wait_ge(edges_in, 32)
                    dve.tensor_copy(e_f[:], e_raw[:]).then_inc(ef_ready, 1)
                    dve.wait_ge(e_turned, 1)
                    dve.tensor_copy(src_i[:], ep[0:ROWS, 0:CHUNKS]).then_inc(e_taken, 1)
                    dve.wait_ge(e_turned, 2)
                    dve.tensor_copy(dst_i[:], ep[0:ROWS, 0:CHUNKS])
                    dve.tensor_copy(dst_f[:], ep[0:ROWS, 0:CHUNKS])
                    dve.wait_ge(kvs_done, TILES + 1)
                    dve.tensor_copy(kv_sum[:], kvs[:, 0:D]).then_inc(kvs_taken, 1)

                @block.scalar
                def _(act):
                    act.wait_ge(ones_ready, SLOTS)
                    with act.Fori(0, ROUNDS) as i:
                        act.wait_ge(veps_ready, i + 1)
                        act.activation(std[:], veps[:], ACT.Sqrt).then_inc(std_ready, 1)
                        for j in range(SLOTS):
                            t = i * SLOTS + j
                            act.wait_ge(turned, t + 1)
                            act.activation(xT[j][:], tp[j % 2][:, 0:256].rearrange("p (k c) -> p k c", k=KD)[:, :, 0:ROWS],
                                           ACT.Copy).then_inc(xT_ready, 1)
                            act.wait_ge(z_done, t + 1)
                            act.activation(at(esed, t), zp[j % 2][0:ROWS, D:D + 2 * HEADS], ACT.Copy
                                           ).then_inc(esed_ready, 1)
                            act.wait_ge(z_stored[j], 16 * i)
                            act.activation(zrow[j][:, :, 0:HD], zp[j % 2][0:ROWS, 0:D].rearrange("p (h c) -> p h c", h=HEADS),
                                           ACT.Copy).then_inc(z_out_ready, 1)

                @block.tensor
                def _(pe):
                    pe.wait_ge(ident_ready, 1)
                    pe.wait_ge(wz_ready, 1)
                    pe.wait_ge(mixw_in, 32)
                    pe.wait_ge(zero_ready, 1)
                    pe.matmul(kvs[:, 0:D], zero_w[:], wkv[:, 0, 0:D], start=True, stop=False)
                    with pe.Fori(0, ROUNDS) as i:
                        for j in range(SLOTS):
                            t = i * SLOTS + j
                            b = j % 2
                            pe.wait_ge(normed, t + 1)
                            pe.wait_ge(xT_ready, bank_free(t, j))
                            for k in range(KD):
                                ins = pe.transpose(tp[b][:, k * 128:k * 128 + ROWS],
                                                   xn[j][:, k * 128:(k + 1) * 128], ident[0:ROWS, 0:ROWS])
                            ins.then_inc(turned, 1)
                            pe.wait_ge(xT_ready, t + 1)
                            pe.wait_ge(z_out_ready, bank_free(t, j))
                            pe.wait_ge(esed_ready, bank_free(t, j))
                            for k in range(KD):
                                ins = pe.matmul(zp[b][0:ROWS, 0:D + 2 * HEADS], xT[j][:, k, :], wz[:, k, :],
                                                start=k == 0, stop=k == KD - 1)
                            ins.then_inc(z_done, 1)
                            pe.wait_ge(kv_ready, bank_free(t, j))
                            for k in range(KD):
                                ins = pe.matmul(kvp[b][0:ROWS, :], xT[j][:, k, :], wkv[:, k, :],
                                                start=k == 0, stop=k == KD - 1)
                            ins.then_inc(kv_done, 1)
                            pe.wait_ge(kv_ready, t + 1)
                            for p in range(2):
                                ins = pe.matmul(kvs[:, p * 128:(p + 1) * 128], kv[j][:, p * 128:(p + 1) * 128],
                                                kv[j][:, D + p * 128:D + (p + 1) * 128], start=False,
                                                stop=False, skip_group_check=True)
                            ins.then_inc(kvs_done, 1)
                    pe.matmul(kvs[:, 0:D], zero_w[:], wkv[:, 0, 0:D], start=False, stop=True
                              ).then_inc(kvs_done, 1)
                    pe.wait_ge(ef_ready, 1)
                    for s in range(2):
                        if s:
                            pe.wait_ge(e_taken, 1)
                        for q in range(EB):
                            ins = pe.transpose(ep[0:ROWS, q * EC:(q + 1) * EC], e_f[:, s, q, :], ident[0:EC, 0:EC])
                        ins.then_inc(e_turned, 1)

        mixer = top.enter_context(ExitStack())
        g_mix = sb(mixer, "g_mix", [128, KD, D])
        gb_mix = sb(mixer, "gb_mix", [ROWS, D])
        x1 = sb(mixer, "x1", [ROWS, TILES, D])

        with ExitStack() as st:
            wq = sb(st, "wq", [128, KD, D])
            wqT = sb(st, "wqT", [128, KD, D])
            bq = sb(st, "bq", [128, KD])
            lg = sb(st, "lg", [128, 2, HD])
            mx = sb(st, "mx", [128, 2])
            nmx = sb(st, "nmx", [128, 2])
            ex = sb(st, "ex", [128, 2, HD])
            rsum = sb(st, "rsum", [128, 2])
            rinv = sb(st, "rinv", [128, 2])
            attn = sb(st, "attn", [128, 2, 128])
            attnT = sb(st, "attnT", [128, 2, 128])
            wqp = bank(st, "wqp")
            atp = bank(st, "atp")
            gp = bank(st, "gp")
            gbp = bank(st, "gbp")
            wq_in, wq_turned, wqT_ready = sem("wq_in"), sem("wq_turned"), sem("wqT_ready")
            nmx_ready, ex_ready, attn_ready = sem("nmx_ready"), sem("ex_ready"), sem("attn_ready")
            attn_turned, attnT_ready, g_done, g_taken = (sem("attn_turned"), sem("attnT_ready"),
                                                         sem("g_done"), sem("g_taken"))
            attn_steps = sem("attn_steps")
            SCALE = HD ** -0.5
            with nc.Block() as block:
                @block.sync
                def _(sp):
                    sp.dma_start(wq[:], w_qkv[:, 0:D].rearrange("(k p) c -> p k c", p=128)).then_inc(wq_in, 16)
                    sp.dma_start(bq[:], b_qkv[0:D].rearrange("(k p) -> p k", p=128)).then_inc(wq_in, 16)

                @block.vector
                def _(dve):
                    step = in_order(dve, attn_steps)
                    halves = [(slice(0, HD), slice(0, HD)), (slice(HD, 128), slice(HD, 128))]
                    for p in range(2):
                        for rows, cols in halves:
                            step(dve.tensor_copy(lg[rows, p, :], kv_sum[rows, p * 128 + cols.start:p * 128 + cols.stop]))
                    step(dve.memset(attn[:], 0.0))
                    step(dve.tensor_reduce(mx[:], lg[:], AX.X, ALU.max))
                    dve.tensor_scalar(nmx[:], mx[:], -SCALE, None, ALU.mult).then_inc(nmx_ready, 1)
                    dve.wait_ge(ex_ready, 2)
                    step(dve.reciprocal(rinv[:], rsum[:]))
                    for p in range(2):
                        for rows, cols in halves:
                            dve.tensor_scalar(attn[rows, p, cols], ex[rows, p, :], rinv[rows, p:p + 1], None,
                                              ALU.mult).then_inc(attn_ready, 1)
                    dve.wait_ge(wq_turned, 1)
                    dve.tensor_copy(wqT[:], wqp[:].rearrange("p (k c) -> p k c", k=KD)).then_inc(wqT_ready, 1)
                    dve.wait_ge(attn_turned, 1)
                    dve.tensor_copy(attnT[:], atp[:, 0:256].rearrange("p (k c) -> p k c", k=2)).then_inc(attnT_ready, 1)
                    dve.wait_ge(g_done, 2)
                    dve.tensor_copy(g_mix[:], gp[:].rearrange("p (k c) -> p k c", k=KD)).then_inc(g_taken, 1)
                    dve.tensor_copy(gb_mix[:], gbp[0:ROWS, 0:D]).then_inc(g_taken, 1)
                    dve.wait_ge(g_taken, 2)

                @block.scalar
                def _(act):
                    act.wait_ge(nmx_ready, 1)
                    for p in range(2):
                        act.activation(ex[:, p, :], lg[:, p, :], ACT.Exp, bias=nmx[:, p:p + 1], scale=SCALE,
                                       accum_out=rsum[:, p:p + 1]).then_inc(ex_ready, 1)

                @block.tensor
                def _(pe):
                    pe.wait_ge(wq_in, 32)
                    for c in range(KD):
                        for i in range(KD):
                            ins = pe.transpose(wqp[:, c * D + i * 128:c * D + (i + 1) * 128],
                                               wq[:, i, c * 128:(c + 1) * 128], ident[:])
                    ins.then_inc(wq_turned, 1)
                    pe.wait_ge(attn_ready, 4)
                    for p in range(2):
                        ins = pe.transpose(atp[:, p * 128:(p + 1) * 128], attn[:, p, :], ident[:])
                    ins.then_inc(attn_turned, 1)
                    pe.wait_ge(attnT_ready, 1)
                    pe.wait_ge(wqT_ready, 1)
                    for i in range(KD):
                        for p in range(2):
                            ins = pe.matmul(gp[:, i * D + p * 128:i * D + (p + 1) * 128],
                                            wqT[:, p, i * 128:(i + 1) * 128], attnT[:, p, :], start=True, stop=True)
                    ins.then_inc(g_done, 1)
                    for p in range(2):
                        ins = pe.matmul(gbp[0:ROWS, p * 128:(p + 1) * 128], bq[:, p:p + 1].to_broadcast([128, ROWS]),
                                        attnT[:, p, :], start=True, stop=True)
                    ins.then_inc(g_done, 1)

        mv1 = sb(mixer, "mv1", [ROWS, TILES, 2])
        rstd1 = sb(mixer, "rstd1", [ROWS, TILES])
        with ExitStack() as st:
            xs = [sb(st, f"m_xs{j}", [ROWS, D]) for j in range(SLOTS)]
            xn = [sb(st, f"m_xn{j}", [ROWS, D]) for j in range(SLOTS)]
            xb = [sb(st, f"m_xb{j}", [ROWS, D]) for j in range(SLOTS)]
            xT = [sb(st, f"m_xT{j}", [128, KD, ROWS]) for j in range(SLOTS)]
            bf2 = sb(st, "bf2", [ROWS, D])
            stats = sb(st, "m_stats", [ROWS, SLOTS, 6])
            mv = sb(st, "m_mv", [ROWS, SLOTS, 2])
            veps = sb(st, "m_veps", [ROWS, TILES])
            std = sb(st, "m_std", [ROWS, TILES])
            wait_carrier = sb(st, "m_carrier", [ROWS, 1])
            tp = [bank(st, f"m_tp{b}") for b in range(2)]
            ap = [bank(st, f"m_ap{b}") for b in range(2)]
            m_in = [sem(f"m_in{j}") for j in range(SLOTS)]
            bf2_in = sem("bf2_in")
            m_turned, m_xT_ready, a_done, x1_ready = sem("m_turned"), sem("m_xT_ready"), sem("a_done"), sem("x1_ready")
            m_steps, m_stat_steps, base_steps, base_ready = (sem("m_steps"), sem("m_stat_steps"),
                                                             sem("base_steps"), sem("base_ready"))
            m_veps_ready, m_std_ready = sem("m_veps_ready"), sem("m_std_ready")
            with nc.Block() as block:
                @block.sync
                def _(sp):
                    def load(t, j):
                        sp.dma_start(xn[j][:], rows_of(xn_dram, t)).then_inc(m_in[j], 16)
                        sp.dma_start(xs[j][:], rows_of(x, t)).then_inc(m_in[j], 16)

                    sp.dma_start(bf2[:], b_fc2.partition_broadcast(ROWS)).then_inc(bf2_in, 16)
                    for j in range(SLOTS):
                        load(j, j)
                    with sp.Fori(1, ROUNDS) as i:
                        for j in range(SLOTS):
                            t = i * SLOTS + j
                            sp.wait_ge(x1_ready, t - SLOTS + 1)
                            sp.wait_ge(base_ready, t - SLOTS + 1)
                            load(t, j)

                @block.tensor
                def _(pe):
                    with pe.Fori(0, ROUNDS) as i:
                        for j in range(SLOTS):
                            t = i * SLOTS + j
                            b = j % 2
                            pe.wait_ge(m_in[j], 32 * i + 32)
                            pe.wait_ge(m_xT_ready, bank_free(t, j))
                            for k in range(KD):
                                ins = pe.transpose(tp[b][:, k * 128:k * 128 + ROWS],
                                                   xn[j][:, k * 128:(k + 1) * 128], ident[0:ROWS, 0:ROWS])
                            ins.then_inc(m_turned, 1)
                            pe.wait_ge(m_xT_ready, t + 1)
                            pe.wait_ge(x1_ready, bank_free(t, j))
                            for k in range(KD):
                                ins = pe.matmul(ap[b][0:ROWS, 0:D], xT[j][:, k, :], g_mix[:, k, :],
                                                start=k == 0, stop=k == KD - 1)
                            ins.then_inc(a_done, 1)

                @block.scalar
                def _(act):
                    with act.Fori(0, ROUNDS) as i:
                        for j in range(SLOTS):
                            act.wait_ge(m_turned, i * SLOTS + j + 1)
                            act.activation(xT[j][:], tp[j % 2][:, 0:256].rearrange("p (k c) -> p k c", k=KD)[:, :, 0:ROWS],
                                           ACT.Copy).then_inc(m_xT_ready, 1)
                    act.wait_ge(m_veps_ready, 1)
                    act.activation(std[:], veps[:], ACT.Sqrt).then_inc(m_std_ready, 1)

                @block.vector
                def _(dve):
                    PER = 3 * SLOTS + 1
                    with dve.Fori(0, ROUNDS) as i:
                        step = in_order(dve, m_steps, PER * i)
                        for j in range(SLOTS):
                            dve.wait_ge(m_in[j], 32 * i + 32)
                            step(dve.tensor_tensor(xb[j][:], xn[j][:], gb_mix[:], ALU.add), wait=j == SLOTS - 1)
                        for j in range(SLOTS):
                            t = i * SLOTS + j
                            dve.wait_ge(a_done, t + 1)
                            dve.tensor_tensor(at(x1, t), ap[j % 2][0:ROWS, 0:D], xb[j][:], ALU.add).then_inc(x1_ready, 1)
                            dve.wait_ge(x1_ready, t + 1)
                            dve.memset(wait_carrier[:], 0.0)
                            step(dve.bn_stats(stats[:, j, :], at(x1, t)), wait=j == SLOTS - 1)
                        dve.memset(wait_carrier[:], 0.0)
                        for j in range(SLOTS):
                            step(dve.bn_aggr(mv[:, j, :], stats[:, j, :]), wait=j == SLOTS - 1)
                        step(dve.tensor_copy(mv1[:, ds(i * SLOTS, SLOTS), :], mv[:]), apart=True)
                    dve.tensor_scalar(veps[:], mv1[:, :, 1], EPS, None, ALU.add).then_inc(m_veps_ready, 1)
                    dve.wait_ge(m_std_ready, 1)
                    dve.reciprocal(rstd1[:], std[:]).then_inc(m_veps_ready, 1)
                    dve.wait_ge(m_veps_ready, 2)

                @block.gpsimd
                def _(pool):
                    pool.wait_ge(bf2_in, 16)
                    with pool.Fori(0, ROUNDS) as i:
                        for j in range(SLOTS):
                            t = i * SLOTS + j
                            pool.wait_ge(m_in[j], 32 * i + 32)
                            pool.tensor_tensor(xs[j][:], xs[j][:], bf2[:], ALU.add).then_inc(base_steps, 1)
                            pool.wait_ge(base_steps, t + 1)
                            pool.wait_ge(x1_ready, t + 1)
                            pool.tensor_tensor(at(total, t), xs[j][:], at(x1, t), ALU.add).then_inc(base_ready, 1)

        with ExitStack() as st:
            h0 = [sb(st, f"h0{j}", [ROWS, D]) for j in range(SLOTS)]
            hT = [sb(st, f"hT{j}", [128, KD, ROWS]) for j in range(SLOTS)]
            hs = [sb(st, f"hs{b}", [128, MB, ROWS]) for b in range(2)]
            wf1 = sb(st, "wf1", [128, KD, MLP])
            wf2 = sb(st, "wf2", [128, MB, D])
            bf1 = sb(st, "bf1", [128, MB])
            gn = sb(st, "gn", [128, KD])
            bn = sb(st, "bn", [128, KD])
            tp = [bank(st, f"f_tp{b}") for b in range(2)]
            hp = [bank(st, f"f_hp{b}") for b in range(4)]
            yp = [bank(st, f"f_yp{b}") for b in range(2)]
            PB = 3
            f_in = sem("f_in")
            h0_ready, f_turned, hT_ready = sem("h0_ready"), sem("f_turned"), sem("hT_ready")
            h_done, h_ready, y_done, y_ready = sem("h_done"), sem("h_ready"), sem("y_done"), sem("y_ready")
            HALF = MB // PB
            with nc.Block() as block:
                @block.sync
                def _(sp):
                    sp.dma_start(wf1[:], w_fc1.rearrange("(k p) c -> p k c", p=128)).then_inc(f_in, 16)
                    sp.dma_start(wf2[:], w_fc2.rearrange("(k p) c -> p k c", p=128)).then_inc(f_in, 16)
                    sp.dma_start(bf1[:], b_fc1.rearrange("(k p) -> p k", p=128)).then_inc(f_in, 16)
                    sp.dma_start(gn[:], norm_g.rearrange("(k p) -> p k", p=128)).then_inc(f_in, 16)
                    sp.dma_start(bn[:], norm_b.rearrange("(k p) -> p k", p=128)).then_inc(f_in, 16)

                @block.vector
                def _(dve):
                    dve.wait_ge(f_in, 80)
                    with dve.Fori(0, ROUNDS) as i:
                        dve.wait_ge(f_turned, i * SLOTS)
                        for j in range(SLOTS):
                            t = i * SLOTS + j
                            dve.tensor_scalar(h0[j][:], at(x1, t), at(mv1, t)[:, 0:1], rstd1[:, ds(t, 1)],
                                              ALU.subtract, ALU.mult).then_inc(h0_ready, 1)
                        for j in range(SLOTS):
                            t = i * SLOTS + j
                            dve.wait_ge(f_turned, t + 1)
                            for k in range(KD):
                                dve.tensor_scalar(hT[j][:, k, :], tp[j % 2][:, k * 128:k * 128 + ROWS],
                                                  gn[:, k:k + 1], bn[:, k:k + 1], ALU.mult, ALU.add).then_inc(hT_ready, 1)
                            dve.wait_ge(y_done, t + 1)
                            dve.tensor_tensor(at(total, t), at(total, t), yp[j % 2][0:ROWS, 0:D], ALU.add
                                              ).then_inc(y_ready, 1)

                @block.scalar
                def _(act):
                    act.wait_ge(f_in, 80)
                    with act.Fori(0, ROUNDS) as i:
                        for j in range(SLOTS):
                            t = i * SLOTS + j
                            act.wait_ge(y_done, bank_free(t, j))
                            for m in range(MB):
                                if m % PB == 0:
                                    act.wait_ge(h_done, t * HALF + m // PB + 1)
                                act.activation(hs[j % 2][:, m, :], hp[(j % 2) * 2 + m // PB][:, (m % PB) * 128:(m % PB) * 128 + ROWS],
                                               ACT.Gelu, bias=bf1[:, m:m + 1]).then_inc(h_ready, 1)

                @block.tensor
                def _(pe):
                    pe.wait_ge(f_in, 80)
                    with pe.Fori(0, ROUNDS) as i:
                        for j in range(SLOTS):
                            t = i * SLOTS + j
                            b = j % 2
                            pe.wait_ge(h0_ready, t + 1)
                            pe.wait_ge(hT_ready, KD * bank_free(t, j))
                            for k in range(KD):
                                ins = pe.transpose(tp[b][:, k * 128:k * 128 + ROWS],
                                                   h0[j][:, k * 128:(k + 1) * 128], ident[0:ROWS, 0:ROWS])
                            ins.then_inc(f_turned, 1)
                            pe.wait_ge(hT_ready, KD * (t + 1))
                            pe.wait_ge(h_ready, MB * bank_free(t, j))
                            for m in range(MB):
                                for k in range(KD):
                                    ins = pe.matmul(hp[b * 2 + m // PB][:, (m % PB) * 128:(m % PB) * 128 + ROWS],
                                                    wf1[:, k, m * 128:(m + 1) * 128], hT[j][:, k, :],
                                                    start=k == 0, stop=k == KD - 1)
                                if m % PB == PB - 1:
                                    ins.then_inc(h_done, 1)
                            pe.wait_ge(y_ready, bank_free(t, j))
                            for m in range(MB):
                                pe.wait_ge(h_ready, t * MB + m + 1)
                                ins = pe.matmul(yp[b][0:ROWS, 0:D], hs[b][:, m, :], wf2[:, m, :],
                                                start=m == 0, stop=m == MB - 1)
                            ins.then_inc(y_done, 1)
        mixer.close()

        K = 4
        GROUPS = CHUNKS // K
        edges = top.enter_context(ExitStack())
        wgt = sb(edges, "wgt", [ROWS, CHUNKS * HEADS])
        scores = edges.enter_context(ExitStack())
        es_e = sb(scores, "es_e", [ROWS, CHUNKS * HEADS])
        ed_e = sb(scores, "ed_e", [ROWS, CHUNKS * HEADS])
        with ExitStack() as st:
            ends = [sb(st, f"ends{b}", [ROWS, 2, K], I32) for b in range(2)]
            got = [sb(st, f"got{b}", [ROWS, 2, K * HEADS]) for b in range(2)]
            ends_ready = sem("ends_ready")
            got_in = [sem(f"got_in{b}") for b in range(2)]
            got_taken = sem("got_taken")
            with nc.Block() as block:
                @block.scalar
                def _(act):
                    with act.Fori(0, GROUPS // 2) as i:
                        for b in range(2):
                            g = i * 2 + b
                            act.wait_ge(got_in[b], 2 * K * 16 * i)
                            for s, e in enumerate((src_i, dst_i)):
                                act.activation(ends[b][:, s, :], e[:, ds(g * K, K)], ACT.Copy).then_inc(ends_ready, 1)

                @block.gpsimd
                def _(pool):
                    with pool.Fori(0, GROUPS // 2) as i:
                        for b in range(2):
                            g = i * 2 + b
                            pool.wait_ge(got_taken, bank_free(g, b))
                            wait_apart(pool, ends_ready, 2 * g + 2)
                            for s, table in enumerate((es_table, ed_table)):
                                for k in range(K):
                                    pool.indirect_dma_start(
                                        got[b][:, s, k * HEADS:(k + 1) * HEADS], None, table,
                                        bass.IndirectOffsetOnAxis(ap=ends[b][:, s, k:k + 1], axis=0)
                                    ).then_inc(got_in[b], 16)

                @block.vector
                def _(dve):
                    with dve.Fori(0, GROUPS // 2) as i:
                        for b in range(2):
                            g = i * 2 + b
                            dve.wait_ge(got_in[b], 2 * K * 16 * (i + 1))
                            dve.tensor_copy(es_e[:, ds(g * K * HEADS, K * HEADS)], got[b][:, 0, :])
                            dve.tensor_copy(ed_e[:, ds(g * K * HEADS, K * HEADS)], got[b][:, 1, :]).then_inc(got_taken, 1)
                    dve.wait_ge(got_taken, GROUPS)

        CB = 25
        BLOCKS = CHUNKS // CB
        SR = HEADS * CB
        carry_f_in = nc.dram_tensor("carry_f_in", (2, HEADS, CHUNKS), F32).ap()
        carry_b_in = nc.dram_tensor("carry_b_in", (2, HEADS, CHUNKS), F32).ap()
        carry_f_out = nc.dram_tensor("carry_f_out", (HEADS, CHUNKS), F32).ap()
        carry_b_out = nc.dram_tensor("carry_b_out", (HEADS, CHUNKS), F32).ap()
        with ExitStack() as st:
            dwin_i = sb(st, "dwin_i", [SR, BLOCKS, ROWS + 2], I32)
            pen = sb(st, "pen", [SR, BLOCKS, ROWS + 1])
            val = sb(st, "val", [SR, BLOCKS, ROWS])
            run_f = sb(st, "run_f", [SR, BLOCKS, ROWS])
            run_b = sb(st, "run_b", [SR, BLOCKS, ROWS])
            link = sb(st, "link", [SR, 2, BLOCKS])
            carry = sb(st, "carry", [HEADS, 2, CHUNKS])
            chain = sb(st, "chain", [HEADS, CHUNKS + 1])
            seed = sb(st, "seed", [SR, BLOCKS])
            best = sb(st, "best", [ROWS, CHUNKS * HEADS])
            tops = sb(st, "tops", [ROWS, CHUNKS * HEADS])
            TB = 4
            tp = [bank(st, f"s_tp{b}") for b in range(BLOCKS // TB)]
            minus_ready, dwin_in, pen_ready = sem("minus_ready"), sem("dwin_in"), sem("pen_ready")
            s_turned, val_ready = sem("s_turned"), sem("val_ready")
            scan_steps = sem("scan_steps")
            link_ready, link_stored, carry_in = sem("link_ready"), sem("link_stored"), sem("carry_in")
            chain_ready, chain_stored, seed_in = sem("chain_ready"), sem("chain_stored"), sem("seed_in")
            run_ready, r_turned, weights_ready = sem("run_ready"), sem("r_turned"), sem("weights_ready")
            gap_ready, blocked = sem("gap_ready"), sem("blocked")
            dst_blocks = dst.rearrange("(b c e) -> c b e", b=BLOCKS, c=CB)
            with nc.Block() as block:
                @block.sync
                def _(sp):
                    sp.wait_ge(minus_ready, 1)
                    for h in range(HEADS):
                        r0, r1 = h * CB, (h + 1) * CB
                        sp.dma_start(dwin_i[r0:r1, :, 1:ROWS + 1], dst_blocks).then_inc(dwin_in, 16)
                        sp.dma_start(dwin_i[r0 + 1:r1, :, 0:1], dst_blocks[0:CB - 1, :, ROWS - 1:ROWS]).then_inc(dwin_in, 16)
                        sp.dma_start(dwin_i[r0:r0 + 1, 1:BLOCKS, 0:1], dst_blocks[CB - 1:CB, 0:BLOCKS - 1, ROWS - 1:ROWS]
                                     ).then_inc(dwin_in, 16)
                        sp.dma_start(dwin_i[r0:r1 - 1, :, ROWS + 1:ROWS + 2], dst_blocks[1:CB, :, 0:1]).then_inc(dwin_in, 16)
                        sp.dma_start(dwin_i[r1 - 1:r1, 0:BLOCKS - 1, ROWS + 1:ROWS + 2], dst_blocks[0:1, 1:BLOCKS, 0:1]
                                     ).then_inc(dwin_in, 16)
                    for way, (c_in, c_out) in enumerate(((carry_f_in, carry_f_out), (carry_b_in, carry_b_out))):
                        sp.wait_ge(link_ready, way + 1)
                        for s in range(2):
                            for h in range(HEADS):
                                sp.dma_start(c_in[s, h].rearrange("(b c) -> c b", c=CB),
                                             link[h * CB:(h + 1) * CB, s, :]).then_inc(link_stored, 16)
                        sp.wait_ge(link_stored, 16 * 2 * HEADS * (way + 1))
                        sp.dma_start(carry[:], c_in.rearrange("s h c -> h s c")).then_inc(carry_in, 16)
                        sp.wait_ge(chain_ready, way + 1)
                        first = way
                        sp.dma_start(c_out, chain[:, first:first + CHUNKS]).then_inc(chain_stored, 16)
                        sp.wait_ge(chain_stored, 16 * (way + 1))
                        for h in range(HEADS):
                            sp.dma_start(seed[h * CB:(h + 1) * CB, :], c_out[h].rearrange("(b c) -> c b", c=CB)).then_inc(seed_in, 16)

                @block.tensor
                def _(pe):
                    pe.wait_ge(blocked, 1)
                    for b in range(BLOCKS):
                        ins = pe.transpose(tp[b // TB][0:SR, (b % TB) * 128:(b % TB) * 128 + ROWS],
                                           best[:, b * SR:(b + 1) * SR],
                                           ident[0:ROWS, 0:ROWS])
                    ins.then_inc(s_turned, 1)
                    pe.wait_ge(run_ready, 1)
                    pe.wait_ge(val_ready, BLOCKS // TB)
                    for b in range(BLOCKS):
                        ins = pe.transpose(tp[b // TB][0:ROWS, (b % TB) * 128:(b % TB) * 128 + SR],
                                           run_b[:, b, :], ident[0:SR, 0:SR])
                    ins.then_inc(r_turned, 1)

                @block.scalar
                def _(act):
                    act.wait_ge(gap_ready, 1)
                    act.activation(wgt[:], wgt[:], ACT.Exp).then_inc(weights_ready, 1)
                    act.wait_ge(weights_ready, 1)

                @block.vector
                def _(dve):
                    step = in_order(dve, scan_steps)
                    dve.memset(dwin_i[:], -1).then_inc(minus_ready, 1)
                    dve.tensor_copy(best[:].rearrange("p (b h c) -> p b h c", b=BLOCKS, h=HEADS),
                                    es_e[:].rearrange("p (b c h) -> p b h c", b=BLOCKS, h=HEADS)).then_inc(blocked, 1)
                    step(dve.memset(chain[:], -BIG))
                    dve.wait_ge(dwin_in, 16 * 5 * HEADS)
                    step(dve.tensor_tensor(pen[:], dwin_i[:, :, 1:ROWS + 2], dwin_i[:, :, 0:ROWS + 1], ALU.not_equal))
                    step(dve.tensor_scalar(pen[:], pen[:], -BIG, None, ALU.mult))
                    dve.wait_ge(s_turned, 1)
                    for q in range(BLOCKS // TB):
                        dve.tensor_copy(val[:, q * TB:(q + 1) * TB, :],
                                        tp[q][0:SR].rearrange("p (b e) -> p b e", b=TB)[:, :, 0:ROWS]).then_inc(val_ready, 1)
                    dve.wait_ge(val_ready, BLOCKS // TB)
                    for way in range(2):
                        back = way == 1
                        source, result = (run_f, run_b) if back else (val, run_f)
                        turn = slice(None, None, -1) if back else slice(None)
                        border = pen[:, :, 1:ROWS + 1] if back else pen[:, :, 0:ROWS]
                        end = 0 if back else ROWS - 1
                        for b in range(BLOCKS):
                            step(dve.tensor_tensor_scan(result[:, b, turn], border[:, b, turn], source[:, b, turn],
                                                        -BIG, ALU.add, ALU.max), wait=b == BLOCKS - 1)
                        step(dve.tensor_copy(link[:, 0, :], result[:, :, end]))
                        dve.tensor_reduce(link[:, 1, :], border, AX.X, ALU.min).then_inc(link_ready, 1)
                        dve.wait_ge(carry_in, 16 * (way + 1))
                        if back:
                            step(dve.memset(chain[:, CHUNKS:CHUNKS + 1], -BIG))
                            dve.tensor_tensor_scan(chain[:, 0:CHUNKS][:, ::-1], carry[:, 1, ::-1], carry[:, 0, ::-1],
                                                   -BIG, ALU.add, ALU.max).then_inc(chain_ready, 1)
                        else:
                            dve.tensor_tensor_scan(chain[:, 1:CHUNKS + 1], carry[:, 1, :], carry[:, 0, :],
                                                   -BIG, ALU.add, ALU.max).then_inc(chain_ready, 1)
                        dve.wait_ge(seed_in, 16 * HEADS * (way + 1))
                        for b in range(BLOCKS):
                            step(dve.tensor_tensor_scan(result[:, b, turn], border[:, b, turn], source[:, b, turn],
                                                        seed[:, b:b + 1], ALU.add, ALU.max), wait=b == BLOCKS - 1)
                    dve.tensor_copy(chain[:, 0:1], chain[:, 0:1]).then_inc(run_ready, 1)
                    step(dve.tensor_tensor(es_e[:], es_e[:], ed_e[:], ALU.add))
                    step(dve.scalar_tensor_tensor(out=wgt[:], in0=es_e[:], scalar=SLOPE, in1=es_e[:], op0=ALU.mult, op1=ALU.max))
                    dve.wait_ge(r_turned, 1)
                    for q in range(BLOCKS // TB):
                        step(dve.tensor_copy(
                            best[:, q * TB * SR:(q + 1) * TB * SR].rearrange("p (b c h) -> p b h c", b=TB, h=HEADS),
                            tp[q][0:ROWS].rearrange("p (b e) -> p b e", b=TB)[:, :, 0:SR].rearrange("p b (h c) -> p b h c", h=HEADS)),
                            wait=q == BLOCKS // TB - 1)
                    step(dve.tensor_tensor(best[:], best[:], ed_e[:], ALU.add))
                    step(dve.scalar_tensor_tensor(out=tops[:], in0=best[:], scalar=SLOPE, in1=best[:], op0=ALU.mult, op1=ALU.max))
                    dve.tensor_tensor(wgt[:], wgt[:], tops[:], ALU.subtract).then_inc(gap_ready, 1)
        scores.close()

        acc = sb(edges, "acc", [ROWS, TILES, ZROW])
        limits = sb(edges, "limits", [1, 2, GROUPS], I32)
        node_row = sb(edges, "node_row", [ROWS, TILES, ROWS])
        with ExitStack() as st:
            dst_g = sb(st, "dst_g", [GROUPS, K * ROWS], I32)
            dst_gf = sb(st, "dst_gf", [GROUPS, K * ROWS])
            extremes = sb(st, "extremes", [GROUPS, 2])
            firsts_i = sb(st, "firsts_i", [GROUPS, TILES - 1], I32)
            firsts = sb(st, "firsts", [GROUPS, TILES - 1])
            passed = sb(st, "passed", [GROUPS, 2, TILES - 1])
            tiles_f = sb(st, "tiles_f", [GROUPS, 2])
            node_i = sb(st, "node_i", [ROWS, TILES, ROWS], I32)
            lp = bank(st, "lp")
            dg_in, firsts_ready, node_i_ready, lim_steps = sem("dg_in"), sem("firsts_ready"), sem("node_i_ready"), sem("lim_steps")
            tiles_ready, tiles_turned = sem("tiles_ready"), sem("tiles_turned")
            with nc.Block() as block:
                @block.sync
                def _(sp):
                    sp.dma_start(dst_g[:], dst.rearrange("(g e) -> g e", g=GROUPS)).then_inc(dg_in, 16)

                @block.gpsimd
                def _(pool):
                    pool.iota(firsts_i[:], [[ROWS, TILES - 1]], base=ROWS, channel_multiplier=0).then_inc(firsts_ready, 1)
                    pool.iota(node_i[:], [[ROWS, TILES], [1, ROWS]], base=0, channel_multiplier=0).then_inc(node_i_ready, 1)

                @block.vector
                def _(dve):
                    step = in_order(dve, lim_steps)
                    dve.wait_ge(dg_in, 16)
                    step(dve.tensor_copy(dst_gf[:], dst_g[:]))
                    step(dve.tensor_reduce(extremes[:, 0:1], dst_gf[:], AX.X, ALU.min))
                    step(dve.tensor_reduce(extremes[:, 1:2], dst_gf[:], AX.X, ALU.max))
                    dve.wait_ge(firsts_ready, 1)
                    step(dve.tensor_copy(firsts[:], firsts_i[:]))
                    for s in range(2):
                        step(dve.tensor_scalar(passed[:, s, :], firsts[:], extremes[:, s:s + 1], None, ALU.is_le))
                    step(dve.tensor_reduce(tiles_f[:], passed[:], AX.X, ALU.add))
                    dve.tensor_scalar(tiles_f[:, 1:2], tiles_f[:, 1:2], 1.0, None, ALU.add).then_inc(tiles_ready, 1)
                    dve.wait_ge(tiles_turned, 1)
                    step(dve.tensor_copy(limits[:], lp[0:1, 0:2 * GROUPS].rearrange("p (s g) -> p s g", s=2)))
                    dve.wait_ge(node_i_ready, 1)
                    step(dve.tensor_copy(node_row[:], node_i[:]))
                    step(dve.memset(acc[:], 0.0))

                @block.tensor
                def _(pe):
                    pe.wait_ge(tiles_ready, 1)
                    for s in range(2):
                        ins = pe.matmul(lp[0:1, s * GROUPS:(s + 1) * GROUPS], tiles_f[:, s:s + 1],
                                        ident[0:GROUPS, 0:GROUPS], start=True, stop=True)
                    ins.then_inc(tiles_turned, 1)

        with ExitStack() as st:
            ZS, WS = 4, 2
            zs = [sb(st, f"zs{s}", [ROWS, K, ZROW]) for s in range(ZS)]
            zw = [sb(st, f"zw{s}", [ROWS, K, ZROW]) for s in range(WS)]
            ids = [sb(st, f"ids{s}", [ROWS, K], I32) for s in range(ZS)]
            onehot = sb(st, "onehot", [ROWS, K, ROWS])
            pp = bank(st, "pp")
            ids_ready, zw_ready = sem("ids_ready"), sem("zw_ready")
            z_in = [sem(f"z_in{s}") for s in range(ZS)]
            onehot_ready, pair_done, acc_done = sem("onehot_ready"), sem("pair_done"), sem("acc_done")
            with nc.Block() as block:
                def tiles_of(eng, g):
                    lo = eng.value_load(limits[0:1, 0, ds(g, 1)], min_val=0, max_val=TILES - 1)
                    hi = eng.value_load(limits[0:1, 1, ds(g, 1)], min_val=1, max_val=TILES)
                    return lo, hi

                @block.scalar
                def _(act):
                    with act.Fori(0, GROUPS // ZS) as i:
                        for s in range(ZS):
                            act.wait_ge(z_in[s], K * 16 * i)
                            act.activation(ids[s][:], src_i[:, ds((i * ZS + s) * K, K)], ACT.Copy).then_inc(ids_ready, 1)

                @block.gpsimd
                def _(pool):

                    def gather(g, s):
                        wait_apart(pool, ids_ready, g + 1)
                        for k in range(K):
                            pool.indirect_dma_start(zs[s][:, k, :], None, z_table,
                                                    bass.IndirectOffsetOnAxis(ap=ids[s][:, k:k + 1], axis=0)
                                                    ).then_inc(z_in[s], 16)

                    for s in range(ZS):
                        gather(s, s)
                    with pool.Fori(1, GROUPS // ZS) as i:
                        for s in range(ZS):
                            g = i * ZS + s
                            pool.wait_ge(zw_ready, g - ZS + 1)
                            gather(g, s)

                @block.vector
                def _(dve):
                    n = dve.alloc_register("dve_pairs")
                    dve.reg_mov(n, 0)
                    with dve.Fori(0, GROUPS // ZS) as i:
                        for s in range(ZS):
                            g = i * ZS + s
                            lo, hi = tiles_of(dve, g)
                            dve.wait_ge(z_in[s], K * 16 * (i + 1))
                            dve.tensor_tensor(zw[s % WS][:].rearrange("p k (h c) -> p (k h) c", h=HEADS),
                                              zs[s][:].rearrange("p k (h c) -> p (k h) c", h=HEADS),
                                              wgt[:, ds(g * K * HEADS, K * HEADS)].unsqueeze(2).to_broadcast([ROWS, K * HEADS, ZW]),
                                              ALU.mult).then_inc(zw_ready, 1)
                            with dve.Fori(lo, hi) as t:
                                dve.tensor_tensor(onehot[:], node_row[:, ds(t, 1), :].to_broadcast([ROWS, K, ROWS]),
                                                  dst_f[:, ds(g * K, K)].unsqueeze(2).to_broadcast([ROWS, K, ROWS]),
                                                  ALU.is_equal).then_inc(onehot_ready, 1)
                                dve.wait_ge(acc_done, dve.snap(n))
                                dve.reg_add(n, n, 1)
                                dve.wait_ge(pair_done, dve.snap(n))
                                dve.tensor_tensor(at(acc, t), at(acc, t), pp[0:ROWS, 0:ZROW], ALU.add).then_inc(acc_done, 1)
                    wait_apart(dve, acc_done, dve.snap(n))

                @block.tensor
                def _(pe):
                    n = pe.alloc_register("pe_pairs")
                    pe.reg_mov(n, 0)
                    with pe.Fori(0, GROUPS // ZS) as i:
                        for s in range(ZS):
                            g = i * ZS + s
                            lo, hi = tiles_of(pe, g)
                            wait_apart(pe, zw_ready, g + 1)
                            with pe.Fori(lo, hi):
                                pe.wait_ge(acc_done, pe.snap(n))
                                pe.reg_add(n, n, 1)
                                pe.wait_ge(onehot_ready, pe.snap(n))
                                for k in range(K):
                                    ins = pe.matmul(pp[0:ROWS, 0:ZROW], onehot[:, k, :], zw[s % WS][:, k, :],
                                                    start=k == 0, stop=k == K - 1)
                                ins.then_inc(pair_done, 1)

        with ExitStack() as st:
            den = sb(st, "den", [ROWS, TILES, HEADS])
            inv = sb(st, "inv", [ROWS, TILES, HEADS])
            norm_steps = sem("norm_steps")
            with nc.Block() as block:
                @block.vector
                def _(dve):
                    step = in_order(dve, norm_steps)
                    heads = acc[:].rearrange("p t (h c) -> p t h c", h=HEADS)
                    step(dve.tensor_scalar(den[:], heads[:, :, :, HD], 0.5, None, ALU.max))
                    step(dve.reciprocal(inv[:], den[:]))
                    for h in range(HEADS):
                        step(dve.tensor_tensor(heads[:, :, h, 0:HD], heads[:, :, h, 0:HD],
                                               inv[:, :, h].unsqueeze(2).to_broadcast([ROWS, TILES, HD]), ALU.mult), wait=h == HEADS - 1)
                    for h in range(HEADS):
                        step(dve.tensor_tensor(total[:, :, h * HD:(h + 1) * HD], total[:, :, h * HD:(h + 1) * HD],
                                               heads[:, :, h, 0:HD], ALU.add), wait=h == HEADS - 1)
        edges.close()

        moe = top.enter_context(ExitStack())
        xf = sb(moe, "xf", [ROWS, TILES, D])
        with ExitStack() as st:
            y0 = [sb(st, f"y0{j}", [ROWS, D]) for j in range(SLOTS)]
            stats = sb(st, "o_stats", [ROWS, SLOTS, 6])
            mv = sb(st, "o_mv", [ROWS, SLOTS, 2])
            veps = sb(st, "o_veps", [ROWS, SLOTS])
            std = sb(st, "o_std", [ROWS, SLOTS])
            rstd = sb(st, "o_rstd", [ROWS, SLOTS])
            o_veps_ready, o_std_ready, o_steps = sem("o_veps_ready"), sem("o_std_ready"), sem("o_steps")
            with nc.Block() as block:
                @block.scalar
                def _(act):
                    with act.Fori(0, 2 * ROUNDS) as i:
                        act.wait_ge(o_veps_ready, i + 1)
                        act.activation(std[:], veps[:], ACT.Sqrt).then_inc(o_std_ready, 1)

                @block.vector
                def _(dve):
                    PER = 2 * (3 * SLOTS + 1)
                    with dve.Fori(0, ROUNDS) as i:
                        step = in_order(dve, o_steps, PER * i)
                        for norm in range(2):
                            def of(j):
                                return at(total, i * SLOTS + j) if norm == 0 else y0[j][:]

                            def to(j):
                                return y0[j][:] if norm == 0 else at(xf, i * SLOTS + j)

                            for j in range(SLOTS):
                                step(dve.bn_stats(stats[:, j, :], of(j)), wait=j == SLOTS - 1, apart=True)
                            for j in range(SLOTS):
                                step(dve.bn_aggr(mv[:, j, :], stats[:, j, :]), wait=j == SLOTS - 1)
                            dve.tensor_scalar(veps[:], mv[:, :, 1], EPS, None, ALU.add).then_inc(o_veps_ready, 1)
                            dve.wait_ge(o_std_ready, 2 * i + norm + 1)
                            step(dve.reciprocal(rstd[:], std[:]))
                            for j in range(SLOTS):
                                step(dve.tensor_scalar(to(j), of(j), mv[:, j, 0:1], rstd[:, j:j + 1],
                                                       ALU.subtract, ALU.mult), wait=j == SLOTS - 1, apart=True)

        gate = sb(moe, "gate", [ROWS, TILES, EXPERTS])
        gam = sb(moe, "gam", [128, KD])
        bet = sb(moe, "bet", [128, KD])
        with ExitStack() as st:
            xin = [sb(st, f"g_xin{j}", [ROWS, D]) for j in range(SLOTS)]
            xfT = [sb(st, f"g_xfT{j}", [128, KD, ROWS]) for j in range(SLOTS)]
            wr = sb(st, "wr", [128, KD, EXPERTS])
            brow = sb(st, "brow", [ROWS, EXPERTS])
            logits = sb(st, "logits", [ROWS, TILES, EXPERTS])
            rest = sb(st, "rest", [ROWS, TILES, EXPERTS])
            hit = sb(st, "hit", [ROWS, TILES, EXPERTS])
            pick = sb(st, "pick", [ROWS, 2, TILES, EXPERTS])
            order_i = sb(st, "order_i", [ROWS, EXPERTS], I32)
            order = sb(st, "order", [ROWS, EXPERTS])
            high = sb(st, "high", [ROWS, 2, TILES])
            low = sb(st, "low", [ROWS, TILES])
            diff = sb(st, "diff", [ROWS, TILES])
            share = sb(st, "share", [ROWS, 2, TILES])
            tp = [bank(st, f"g_tp{b}") for b in range(2)]
            gl = [bank(st, f"g_gl{b}") for b in range(2)]
            g_in, xin_ready, g_turned, xfT_ready = sem("g_in"), sem("xin_ready"), sem("g_turned"), sem("xfT_ready")
            gl_done, logits_ready, order_ready = sem("gl_done"), sem("logits_ready"), sem("order_ready")
            gate_steps, diff_ready, second_ready = sem("gate_steps"), sem("diff_ready"), sem("second_ready")
            with nc.Block() as block:
                @block.sync
                def _(sp):
                    sp.dma_start(wr[:], Wr.rearrange("(k p) e -> p k e", p=128)).then_inc(g_in, 16)
                    sp.dma_start(brow[:], br.partition_broadcast(ROWS)).then_inc(g_in, 16)
                    sp.dma_start(gam[:], gamma.rearrange("(k p) -> p k", p=128)).then_inc(g_in, 16)
                    sp.dma_start(bet[:], beta.rearrange("(k p) -> p k", p=128)).then_inc(g_in, 16)

                @block.gpsimd
                def _(pool):
                    pool.iota(order_i[:], [[1, EXPERTS]], base=0, channel_multiplier=0).then_inc(order_ready, 1)

                @block.scalar
                def _(act):
                    with act.Fori(0, ROUNDS) as i:
                        act.wait_ge(g_turned, i * SLOTS)
                        for j in range(SLOTS):
                            act.activation(xin[j][:], at(xf, i * SLOTS + j), ACT.Copy).then_inc(xin_ready, 1)
                    act.wait_ge(diff_ready, 1)
                    act.activation(low[:], diff[:], ACT.Exp).then_inc(second_ready, 1)

                @block.tensor
                def _(pe):
                    pe.wait_ge(g_in, 64)
                    with pe.Fori(0, ROUNDS) as i:
                        for j in range(SLOTS):
                            t = i * SLOTS + j
                            b = j % 2
                            pe.wait_ge(xin_ready, t + 1)
                            pe.wait_ge(xfT_ready, KD * bank_free(t, j))
                            for k in range(KD):
                                ins = pe.transpose(tp[b][:, k * 128:k * 128 + ROWS],
                                                   xin[j][:, k * 128:(k + 1) * 128], ident[0:ROWS, 0:ROWS])
                            ins.then_inc(g_turned, 1)
                            pe.wait_ge(xfT_ready, KD * (t + 1))
                            pe.wait_ge(logits_ready, bank_free(t, j))
                            for k in range(KD):
                                ins = pe.matmul(gl[b][0:ROWS, 0:EXPERTS], xfT[j][:, k, :], wr[:, k, :],
                                                start=k == 0, stop=k == KD - 1)
                            ins.then_inc(gl_done, 1)

                @block.vector
                def _(dve):
                    dve.wait_ge(g_in, 64)
                    with dve.Fori(0, ROUNDS) as i:
                        for j in range(SLOTS):
                            t = i * SLOTS + j
                            dve.wait_ge(g_turned, t + 1)
                            for k in range(KD):
                                dve.tensor_scalar(xfT[j][:, k, :], tp[j % 2][:, k * 128:k * 128 + ROWS],
                                                  gam[:, k:k + 1], bet[:, k:k + 1], ALU.mult, ALU.add).then_inc(xfT_ready, 1)
                            dve.wait_ge(gl_done, t + 1)
                            dve.tensor_tensor(at(logits, t), gl[j % 2][0:ROWS, 0:EXPERTS], brow[:], ALU.add
                                              ).then_inc(logits_ready, 1)
                    dve.wait_ge(logits_ready, TILES)
                    step = in_order(dve, gate_steps)
                    dve.wait_ge(order_ready, 1)
                    step(dve.tensor_copy(order[:], order_i[:]))
                    step(dve.tensor_scalar(order[:], order[:], -float(EXPERTS), None, ALU.add))
                    orders = order[:].unsqueeze(1).to_broadcast([ROWS, TILES, EXPERTS])
                    for r in range(2):
                        of = logits if r == 0 else rest
                        step(dve.tensor_reduce(high[:, r, :], of[:], AX.X, ALU.max))
                        step(dve.tensor_tensor(hit[:], of[:], high[:, r, :].unsqueeze(2).to_broadcast([ROWS, TILES, EXPERTS]), ALU.is_equal))
                        step(dve.tensor_tensor(hit[:], hit[:], orders, ALU.mult))
                        step(dve.tensor_reduce(low[:], hit[:], AX.X, ALU.min))
                        step(dve.tensor_tensor(pick[:, r], orders, low[:].unsqueeze(2).to_broadcast([ROWS, TILES, EXPERTS]), ALU.is_equal))
                        if r == 0:
                            step(dve.scalar_tensor_tensor(out=rest[:], in0=pick[:, 0], scalar=-BIG, in1=logits[:], op0=ALU.mult, op1=ALU.add))
                    dve.tensor_tensor(diff[:], high[:, 1, :], high[:, 0, :], ALU.subtract).then_inc(diff_ready, 1)
                    dve.wait_ge(second_ready, 1)
                    step(dve.tensor_scalar(diff[:], low[:], 1.0, None, ALU.add))
                    step(dve.reciprocal(share[:, 0, :], diff[:]))
                    step(dve.tensor_tensor(share[:, 1, :], low[:], share[:, 0, :], ALU.mult))
                    for r in range(2):
                        step(dve.tensor_tensor(pick[:, r], pick[:, r], share[:, r, :].unsqueeze(2).to_broadcast([ROWS, TILES, EXPERTS]), ALU.mult))
                    step(dve.tensor_tensor(gate[:], pick[:, 0], pick[:, 1], ALU.add))

        with ExitStack() as st:
            ES = 2
            xin = [sb(st, f"e_xin{j}", [ROWS, D]) for j in range(SLOTS)]
            xfT = [sb(st, f"e_xfT{j}", [128, KD, ROWS]) for j in range(SLOTS)]
            hs = [sb(st, f"e_hs{b}", [ROWS, HID]) for b in range(ES)]
            hT = [sb(st, f"e_hT{b}", [128, HB, ROWS]) for b in range(ES)]
            w1s = sb(st, "w1s", [128, EXPERTS, KD, HID])
            w2s = sb(st, "w2s", [128, EXPERTS, HB, D])
            b1s = sb(st, "b1s", [1, EXPERTS, HID])
            b2s = sb(st, "b2s", [1, EXPERTS, D])
            ones = sb(st, "ones", [1, ROWS])
            tp = bank(st, "e_tp")
            hp = [bank(st, f"e_hp{b}") for b in range(ES)]
            htp = [bank(st, f"e_htp{b}") for b in range(ES)]
            yp = [bank(st, f"e_yp{b}") for b in range(ES)]
            w_in, ones_set = sem("w_in"), sem("ones_set")
            e_xin_ready, e_turned2, e_xfT_ready = sem("e_xin_ready"), sem("e_turned2"), sem("e_xfT_ready")
            e_h_done, e_h_ready, e_ht_done, e_hT_ready = sem("e_h_done"), sem("e_h_ready"), sem("e_ht_done"), sem("e_hT_ready")
            e_y_done, e_y_added = sem("e_y_done"), sem("e_y_added")
            out_stored = [sem(f"out_stored{j}") for j in range(SLOTS)]
            with nc.Block() as block:
                @block.sync
                def _(sp):
                    for e in range(EXPERTS):
                        sp.dma_start(w1s[:, e], W1[e].rearrange("(k p) c -> p k c", p=128)).then_inc(w_in, 16)
                        sp.dma_start(w2s[:, e], W2[e].rearrange("(k p) c -> p k c", p=128)).then_inc(w_in, 16)
                    sp.dma_start(b1s[:], b1.rearrange("(a e) c -> a e c", a=1)).then_inc(w_in, 16)
                    sp.dma_start(b2s[:], b2.rearrange("(a e) c -> a e c", a=1)).then_inc(w_in, 16)
                    with sp.Fori(0, ROUNDS) as i:
                        for j in range(SLOTS):
                            t = i * SLOTS + j
                            sp.wait_ge(e_y_added, EXPERTS * (t + 1))
                            sp.dma_start(rows_of(out, t), at(total, t)).then_inc(out_stored[j], 16)
                    for j in range(SLOTS):
                        sp.wait_ge(out_stored[j], 16 * ROUNDS)

                @block.scalar
                def _(act):
                    with act.Fori(0, ROUNDS) as i:
                        for j in range(SLOTS):
                            t = i * SLOTS + j
                            act.wait_ge(e_turned2, t)
                            act.activation(xin[j][:], at(xf, t), ACT.Copy).then_inc(e_xin_ready, 1)
                            with act.Fori(0, EXPERTS // ES) as r:
                                for b in range(ES):
                                    n = (t * (EXPERTS // ES) + r) * ES + b
                                    act.wait_ge(e_h_done, n + 1)
                                    act.activation(hs[b][:], hp[b][0:ROWS, :], ACT.Gelu).then_inc(e_h_ready, 1)

                @block.vector
                def _(dve):
                    with dve.Fori(0, ROUNDS) as i:
                        for j in range(SLOTS):
                            t = i * SLOTS + j
                            dve.wait_ge(e_turned2, t + 1)
                            for k in range(KD):
                                dve.tensor_scalar(xfT[j][:, k, :], tp[:, k * 128:k * 128 + ROWS],
                                                  gam[:, k:k + 1], bet[:, k:k + 1], ALU.mult, ALU.add).then_inc(e_xfT_ready, 1)
                            with dve.Fori(0, EXPERTS // ES) as r:
                                for b in range(ES):
                                    n = (t * (EXPERTS // ES) + r) * ES + b
                                    dve.wait_ge(e_ht_done, n + 1)
                                    dve.tensor_copy(hT[b][:], htp[b][:].rearrange("p (m c) -> p m c", m=HB)[:, :, 0:ROWS]
                                                    ).then_inc(e_hT_ready, 1)
                                    dve.wait_ge(e_y_done, n + 1)
                                    dve.wait_ge(e_y_added, n)
                                    dve.scalar_tensor_tensor(out=at(total, t), in0=yp[b][0:ROWS, 0:D],
                                                             scalar=at(gate, t)[:, ds(r * ES + b, 1)], in1=at(total, t),
                                                             op0=ALU.mult, op1=ALU.add).then_inc(e_y_added, 1)

                @block.gpsimd
                def _(pool):
                    pool.memset(ones[:], 1.0).then_inc(ones_set, 1)

                @block.tensor
                def _(pe):
                    pe.wait_ge(w_in, 16 * (2 * EXPERTS + 2))
                    pe.wait_ge(ones_set, 1)
                    with pe.Fori(0, ROUNDS) as i:
                        for j in range(SLOTS):
                            t = i * SLOTS + j
                            pe.wait_ge(e_xin_ready, t + 1)
                            for k in range(KD):
                                ins = pe.transpose(tp[:, k * 128:k * 128 + ROWS],
                                                   xin[j][:, k * 128:(k + 1) * 128], ident[0:ROWS, 0:ROWS])
                            ins.then_inc(e_turned2, 1)
                            wait_apart(pe, e_xfT_ready, KD * (t + 1))
                            with pe.Fori(0, EXPERTS // ES) as r:
                                for b in range(ES):
                                    e = r * ES + b
                                    n = (t * (EXPERTS // ES) + r) * ES + b
                                    pe.matmul(hp[b][0:ROWS, :], ones[:], b1s[:, ds(e, 1), :].rearrange("p a c -> p (a c)"),
                                              start=True, stop=False)
                                    for k in range(KD):
                                        ins = pe.matmul(hp[b][0:ROWS, :], xfT[j][:, k, :],
                                                        w1s[:, ds(e, 1), k, :].rearrange("p a c -> p (a c)"),
                                                        start=False, stop=k == KD - 1)
                                    ins.then_inc(e_h_done, 1)
                                for b in range(ES):
                                    e = r * ES + b
                                    n = (t * (EXPERTS // ES) + r) * ES + b
                                    pe.wait_ge(e_h_ready, n + 1)
                                    for m in range(HB):
                                        ins = pe.transpose(htp[b][:, m * 128:m * 128 + ROWS],
                                                           hs[b][:, m * 128:(m + 1) * 128], ident[0:ROWS, 0:ROWS])
                                    ins.then_inc(e_ht_done, 1)
                                for b in range(ES):
                                    e = r * ES + b
                                    n = (t * (EXPERTS // ES) + r) * ES + b
                                    pe.matmul(yp[b][0:ROWS, 0:D], ones[:], b2s[:, ds(e, 1), :].rearrange("p a c -> p (a c)"),
                                              start=True, stop=False)
                                    pe.wait_ge(e_hT_ready, n + 1)
                                    for m in range(HB):
                                        ins = pe.matmul(yp[b][0:ROWS, 0:D], hT[b][:, m, :],
                                                        w2s[:, ds(e, 1), m, :].rearrange("p a c -> p (a c)"),
                                                        start=False, stop=m == HB - 1)
                                    ins.then_inc(e_y_done, 1)
                                wait_apart(pe, e_y_added, (t * (EXPERTS // ES) + r + 1) * ES)
        moe.close()
    return nc


_INS = ['x', 'src', 'dst', 'L0_gnn_W', 'L0_gnn_a_src', 'L0_gnn_a_dst', 'L0_mix_w_qkv', 'L0_mix_b_qkv',
        'L0_mix_norm_g', 'L0_mix_norm_b', 'L0_mix_w_fc1', 'L0_mix_b_fc1', 'L0_mix_w_fc2', 'L0_mix_b_fc2',
        'L0_ffn_gamma', 'L0_ffn_beta', 'L0_ffn_Wr', 'L0_ffn_br', 'L0_ffn_W1', 'L0_ffn_b1', 'L0_ffn_W2',
        'L0_ffn_b2']
_OUTS = [((3125, 256), 'float32')]


def kernel(**inputs):
    import numpy as _np
    import concourse.bacc as _bacc
    from concourse import mybir as _mybir
    from concourse.bass_utils import run_bass_kernel_spmd as _run

    nc = _bacc.Bacc("TRN2", target_bir_lowering=False, num_devices=1)
    arrays, args = {}, []
    for name in _INS:
        a = _np.ascontiguousarray(inputs[name])
        arrays[f"in_{name}_dram"] = a
        args.append(nc.dram_tensor(f"in_{name}_dram", a.shape, _mybir.dt.from_np(a.dtype), kind="ExternalInput").ap())
    for i, (shape, dtype) in enumerate(_OUTS):
        dt = _mybir.dt.from_np(_np.dtype(dtype))
        args.append(nc.dram_tensor(f"out_{i}_dram", shape, dt, kind="ExternalOutput").ap())
    gps_layer_kernel(nc, *args)
    r = _run(nc, [arrays], core_ids=[0])
    got = tuple(r.results[0][f"out_{i}_dram"] for i in range(len(_OUTS)))
    return got[0]
```
